# Optimizing a Trainium2 kernel written in Bass

```python
import numpy as np
import jax
import jax.numpy as jnp

def _softmax(x, axis=-1):
    return jax.nn.softmax(x, axis=axis)
def _gelu(x):
    return jax.nn.gelu(x, approximate=True)
def _silu(x):
    return jax.nn.silu(x)
def _sigmoid(x):
    return jax.nn.sigmoid(x)
def _layernorm(x, axis=-1, eps=1e-5):
    m = jnp.mean(x, axis=axis, keepdims=True)
    v = jnp.var(x, axis=axis, keepdims=True)
    return (x - m) / jnp.sqrt(v + eps)
def _scatter_add(tgt, idx, src, axis=0):
    return tgt.at[idx].add(src)
def _segment_sum(src, seg, n):
    return jax.ops.segment_sum(src, seg, n)

kernel_name = 'mk_rec_standalone_d1_rec_724ae1'

def setup_inputs(seed: int = 0):
    np.random.seed(seed)
    _w = jnp.asarray
    def _rec_inputs():
        import jax
        import jax.numpy as jnp
        _rk = jax.random.key(seed)
        r_feature_emb = 7.22013e-05 + 1.00017 * jax.random.normal(jax.random.fold_in(_rk, 1), (4096, 32, 64), jnp.float32)
        return r_feature_emb
    r_feature_emb = _rec_inputs()
    def _L0_rec_setup():
        import jax, jax.numpy as jnp
        import numpy as np
        from itertools import combinations
        NUM_FIELDS = 32
        EMBED = 64
        PAIRS = np.array(list(combinations(range(NUM_FIELDS), 2)), dtype=np.int32)
        key = jax.random.key(seed)
        k1, k2 = jax.random.split(key)
        feature_emb = jax.random.normal(k1, (4096, NUM_FIELDS, EMBED), dtype=jnp.float32)
        W = jax.random.normal(k2, (PAIRS.shape[0], EMBED, EMBED), dtype=jnp.float32) * (1.0 / np.sqrt(EMBED))
        return {'feature_emb': feature_emb, 'W': W}
    _L0_rec_all = _L0_rec_setup()
    _L0_rec_in = {k: v for k, v in _L0_rec_all.items() if k in ('W', )}
    del _L0_rec_all

    return {
        "r_feature_emb": r_feature_emb,
        "L0_rec_W": _L0_rec_in["W"],
    }

def reference(r_feature_emb, L0_rec_W):
    import jax
    import jax.numpy as jnp
    def _L0_rec_ref(feature_emb, W):
        import jax, jax.numpy as jnp
        import numpy as np
        from itertools import combinations
        NUM_FIELDS = 32
        EMBED = 64
        PAIRS = np.array(list(combinations(range(NUM_FIELDS), 2)), dtype=np.int32)
        idx_i = jnp.asarray(PAIRS[:, 0])
        idx_j = jnp.asarray(PAIRS[:, 1])
        v_i = feature_emb[:, idx_i, :]
        v_j = feature_emb[:, idx_j, :]
        proj = jnp.einsum('bpe,pfe->bpf', v_i, W)
        return proj * v_j

    y = _L0_rec_ref(r_feature_emb, L0_rec_W)
    return y


_drawn_inputs = setup_inputs


def setup_inputs(seed=0):
    import zlib

    import numpy as np

    out = dict(_drawn_inputs(seed))
    spreads = {}
    factors = {}
    for name, (base, spread) in spreads.items():
        noise = np.random.default_rng([zlib.crc32(name.encode()), seed]).standard_normal(out[name].shape)
        drawn = base * np.exp(spread * noise) if base else spread * noise
        out[name] = jnp.asarray(drawn.astype(out[name].dtype))
    for name, factor in factors.items():
        out[name] = (out[name] * factor).astype(out[name].dtype)
    return out
```

```python
from contextlib import ExitStack

import concourse.bass as bass
from concourse import mybir

F32 = mybir.dt.float32
F32R = mybir.dt.float32r
MULT = mybir.AluOpType.mult
SUBTRACT = mybir.AluOpType.subtract
NOT_EQUAL = mybir.AluOpType.not_equal
COPY = mybir.ActivationFunctionType.Copy

P = 128
BATCH, FIELDS, EMBED = 4096, 32, 64
TILES = BATCH // P
PAIRS = FIELDS * (FIELDS - 1) // 2
COLS = PAIRS * EMBED
BANK = 512

HALF = 512
CHUNK = 2 * HALF
CHUNKS = COLS // CHUNK

UNIT_PAIRS = 24
UNIT_COLS = UNIT_PAIRS * EMBED
PSUM_SLOTS = 2
STAGES = 5
RAW_SLOTS = 5

GROUPS = FIELDS // 2
TURN_SLOTS = 2
XT_SLOTS = 4

AHEAD_GROUP = 2
AHEAD_W = 3
SPLIT_LOWER_AT = 20
SPLIT_UPPER_AT = 1


def first_pair(i):
    return i * (FIELDS - 1) - i * (i - 1) // 2


def plan():
    units = []
    for i in range(FIELDS - 1):
        pairs = FIELDS - 1 - i
        if pairs > UNIT_PAIRS:
            first = (pairs + 1) // 2
            units += [[(i, i + 1, first)], [(i, i + 1 + first, pairs - first)]]
        elif sum(p[2] for p in units[-1]) + pairs <= UNIT_PAIRS and pairs < UNIT_PAIRS // 2 + 1:
            units[-1].append((i, i + 1, pairs))
        else:
            units.append([(i, i + 1, pairs)])
    start = [first_pair(u[0][0]) + u[0][1] - u[0][0] - 1 for u in units] + [PAIRS]
    return [(u, s * EMBED, (e - s) * EMBED) for u, s, e in zip(units, start, start[1:])]


UNITS = plan()
N = len(UNITS)
assert N % PSUM_SLOTS == 0 and N % STAGES == 0 and GROUPS % XT_SLOTS == 0
ROUNDS = N // STAGES

FIRST_UNIT_OF_GROUP = [min(u for u in range(N) for p in UNITS[u][0] if p[0] // 2 == g)
                       for g in range(GROUPS)]
LAST_UNIT_OF_GROUP = [max(u for u in range(N) for p in UNITS[u][0] if p[0] // 2 == g)
                      for g in range(GROUPS)]
FIRST_UNIT_OF_CHUNK = [max(u for u in range(N) if UNITS[u][1] <= k * CHUNK) for k in range(CHUNKS)]
LAST_CHUNK_OF_UNIT = [(UNITS[u][1] + UNITS[u][2] - 1) // CHUNK for u in range(N)]


def groups_asked_at(u):
    ahead, v = divmod(u + AHEAD_GROUP, N)
    return [(ahead, g) for g in range(GROUPS) if FIRST_UNIT_OF_GROUP[g] == v]


assert SPLIT_LOWER_AT >= FIRST_UNIT_OF_GROUP[GROUPS // 2 - 1] - AHEAD_GROUP


def groups_asked_before():
    return [g for g in range(GROUPS) if FIRST_UNIT_OF_GROUP[g] < AHEAD_GROUP]


def chunks_asked_at(u):
    return [k for k in range(CHUNKS) if max(FIRST_UNIT_OF_CHUNK[k] - AHEAD_W, 0) == u]


def group_fields(g):
    return [i for i in (2 * g, 2 * g + 1) if i < FIELDS - 1]


def matmul_pieces(unit, start):
    pieces, col = [], 0
    for i, _, pairs in unit:
        end, stretches = col + pairs * EMBED, []
        while col < end:
            n = min(end, (col // BANK + 1) * BANK) - col
            stretches.append((col, start + col, n))
            col += n
        pieces.append((i, stretches))
    return pieces


def build(nc, x, wt, out):
    with ExitStack() as ctx:
        def sbuf(name, shape, dtype=F32):
            return ctx.enter_context(nc.sbuf_tensor(name, shape, dtype))

        def psum(name, cols):
            return ctx.enter_context(nc.psum_tensor(name, [P, cols], F32))

        def sem(name):
            return ctx.enter_context(nc.semaphore(name))

        w = sbuf("w", [P, COLS], F32R)
        w_raw = sbuf("w_raw", [P, RAW_SLOTS, HALF])
        x_rows = sbuf("x_rows", [P, 2, FIELDS * EMBED])
        x_parts = sbuf("x_parts", [P, FIELDS, 2, EMBED], F32R)
        x_turned = sbuf("x_turned", [P, XT_SLOTS, 2, 2, P], F32R)
        stage = sbuf("stage", [P, STAGES, UNIT_COLS])
        identity = sbuf("identity", [P, P])
        products = [psum(f"products{s}", UNIT_COLS) for s in range(PSUM_SLOTS)]
        turned = [psum(f"turned{s}", BANK)[:, 0:2 * P].rearrange("p (i b) -> p i b", i=2)
                  for s in range(TURN_SLOTS)]

        x_landed = [sem(f"x_landed{s}") for s in range(2)]
        w_landed = [sem(f"w_landed{s}") for s in range(RAW_SLOTS)]
        identity_zeroed = sem("identity_zeroed")
        identity_ready = sem("identity_ready")
        w_high_ready = sem("w_high_ready")
        w_low_ready = sem("w_low_ready")
        x_high_ready = sem("x_high_ready")
        x_low_ready = sem("x_low_ready")
        group_turned = sem("group_turned")
        group_ready = sem("group_ready")
        unit_multiplied = sem("unit_multiplied")
        unit_done = sem("unit_done")
        stored = [sem(f"stored{s}") for s in range(STAGES)]

        block = ctx.enter_context(nc.Block())

        def over_tiles(engine, step):
            step(0, 0, True, False)
            with engine.Fori(0, (TILES - 2) // 2) as n:
                step(2 * n + 1, 1, False, False)
                step(2 * n + 2, 0, False, False)
            step(TILES - 1, 1, False, True)

        def x_landings(t, buffer):
            return (t - buffer) * 8 + 16

        @block.sync
        def _(sp):
            def load_x(t, buffer):
                sp.dma_start(x_rows[:, buffer, :], x[bass.ds(t * P, P), :]).then_inc(x_landed[buffer], 16)

            def load_w(k):
                if k >= RAW_SLOTS:
                    sp.wait_ge(w_low_ready, k - RAW_SLOTS + 1)
                sp.dma_start(w_raw[:, k % RAW_SLOTS, :], wt[:, k * HALF:(k + 1) * HALF]) \
                    .then_inc(w_landed[k % RAW_SLOTS], 16)

            def tile(t, buffer, first, last):
                for u, (_, start, cols) in enumerate(UNITS):
                    if first:
                        for k in chunks_loaded_at(u):
                            load_w(k)
                    sp.wait_ge(unit_done, t * N + u + 1)
                    sp.dma_start(out[bass.ds(t * P, P), start:start + cols], stage[:, u % STAGES, 0:cols]) \
                        .then_inc(stored[u % STAGES], 16)
                    if u == 0 and not last:
                        load_x(t + 1, 1 - buffer)

            def chunks_loaded_at(u):
                return [k + RAW_SLOTS for k in chunks_asked_at(u) if k + RAW_SLOTS < CHUNKS]

            load_x(0, 0)
            for k in range(RAW_SLOTS):
                load_w(k)
            over_tiles(sp, tile)
            for s in range(STAGES):
                sp.wait_ge(stored[s], 16 * ROUNDS * TILES)

        @block.gpsimd
        def _(pool):
            nc.gpsimd.memset(identity[:, :], 0.0).then_inc(identity_zeroed, 1)
            pool.wait_ge(identity_zeroed, 1)
            nc.gpsimd.affine_select(out=identity[:, :], in_=identity[:, :], compare_op=NOT_EQUAL, fill=1.0,
                                    base=0, pattern=[[-1, P]], channel_multiplier=1).then_inc(identity_ready, 1)

            def split_low(t, buffer, half):
                a, b = half * FIELDS // 2, (half + 1) * FIELDS // 2
                pool.wait_ge(x_high_ready, 2 * t + half + 1)
                nc.gpsimd.tensor_tensor(
                    x_parts[:, a:b, 1, :].bitcast(F32),
                    x_rows[:, buffer, a * EMBED:b * EMBED].rearrange("p (i e) -> p i e", e=EMBED),
                    x_parts[:, a:b, 0, :].bitcast(F32), SUBTRACT).then_inc(x_low_ready, 1)

            def tile(t, buffer, first, last):
                split_low(t, buffer, 1)
                if not last:
                    split_low(t + 1, 1 - buffer, 0)

            split_low(0, 0, 0)
            over_tiles(pool, tile)

        @block.scalar
        def _(act):
            def split_high(t, buffer, half, first):
                a, b = half * FIELDS // 2, (half + 1) * FIELDS // 2
                act.wait_ge(x_landed[buffer], x_landings(t, buffer))
                if not first:
                    act.wait_ge(group_turned, (t - 1) * GROUPS + (half + 1) * GROUPS // 2)
                nc.scalar.activation(
                    x_parts[:, a:b, 0, :],
                    x_rows[:, buffer, a * EMBED:b * EMBED].rearrange("p (i e) -> p i e", e=EMBED),
                    COPY).then_inc(x_high_ready, 1)

            def evacuate(t, g, first):
                act.wait_ge(group_turned, t * GROUPS + g + 1)
                if not first:
                    behind, before = divmod(g - XT_SLOTS, GROUPS)
                    act.wait_ge(unit_multiplied, (t + behind) * N + LAST_UNIT_OF_GROUP[before] + 1)
                n = len(group_fields(g))
                high, low = slice(0, EMBED), slice(EMBED, P)
                for rows, swapped, source in ((slice(0, P), 0, slice(0, P)), (high, 1, low), (low, 1, high)):
                    nc.scalar.activation(x_turned[rows, g % XT_SLOTS, swapped, 0:n, :],
                                         turned[g % TURN_SLOTS][source, 0:n, :], COPY) \
                        .then_inc(group_ready, 1)

            def round_w(k):
                act.wait_ge(w_landed[k % RAW_SLOTS], 16 * (k // RAW_SLOTS + 1))
                for half in range(2):
                    rows = slice(half * EMBED, (half + 1) * EMBED)
                    c = k * CHUNK + half * HALF
                    nc.scalar.activation(w[rows, c:c + HALF], w_raw[rows, k % RAW_SLOTS, :], COPY) \
                        .then_inc(w_high_ready, 1)

            def tile(t, buffer, first, last):
                for u in range(N):
                    for ahead, g in groups_asked_at(u):
                        if not (last and ahead):
                            evacuate(t + ahead, g, first and not ahead and g < XT_SLOTS)
                    if first:
                        for k in chunks_asked_at(u):
                            round_w(k)
                    if u == SPLIT_UPPER_AT:
                        split_high(t, buffer, 1, first)
                    if u == SPLIT_LOWER_AT and not last:
                        split_high(t + 1, 1 - buffer, 0, False)

            split_high(0, 0, 0, True)
            for g in groups_asked_before():
                evacuate(0, g, True)
            over_tiles(act, tile)

        @block.tensor
        def _(pe):
            def transpose(t, g, first):
                if g == 0 or g == GROUPS // 2:
                    pe.wait_ge(x_low_ready, 2 * t + (g > 0) + 1)
                if not first or g >= TURN_SLOTS:
                    pe.wait_ge(group_ready, 3 * (t * GROUPS + g - TURN_SLOTS + 1))
                for n, i in enumerate(group_fields(g)):
                    parts = x_parts[:, i, :, :].bitcast(F32).rearrange("p s e -> p (s e)")
                    last = nc.tensor.transpose(turned[g % TURN_SLOTS][:, n, :], parts, identity[:, :])
                last.then_inc(group_turned, 1)

            def multiply(t, u, first):
                unit, start, _ = UNITS[u]
                for g in range(GROUPS):
                    if FIRST_UNIT_OF_GROUP[g] == u:
                        pe.wait_ge(group_ready, 3 * (t * GROUPS + g + 1))
                if first:
                    pe.wait_ge(w_low_ready, LAST_CHUNK_OF_UNIT[u] + 1)
                if not first or u >= PSUM_SLOTS:
                    pe.wait_ge(unit_done, t * N + u - PSUM_SLOTS + 1)
                slot = products[u % PSUM_SLOTS]
                for i, stretches in matmul_pieces(unit, start):
                    for swapped in range(2):
                        weights = x_turned[:, i // 2 % XT_SLOTS, swapped, i % 2, :]
                        for c, wc, n in stretches:
                            last = nc.tensor.matmul(slot[:, c:c + n], weights, w[:, wc:wc + n],
                                                    start=(swapped == 0), stop=(swapped == 1))
                last.then_inc(unit_multiplied, 1)

            def tile(t, buffer, first, last):
                for u in range(N):
                    for ahead, g in groups_asked_at(u):
                        if not (last and ahead):
                            transpose(t + ahead, g, first and not ahead)
                    multiply(t, u, first)

            pe.wait_ge(identity_ready, 1)
            for g in groups_asked_before():
                transpose(0, g, True)
            over_tiles(pe, tile)

        @block.vector
        def _(dve):
            def split_w_low(k):
                for half in range(2):
                    rows = slice(half * EMBED, (half + 1) * EMBED)
                    across = slice((1 - half) * EMBED, (2 - half) * EMBED)
                    c = k * CHUNK + half * HALF
                    dve.wait_ge(w_high_ready, 2 * k + half + 1)
                    last = nc.vector.tensor_tensor(w[across, c:c + HALF], w_raw[rows, k % RAW_SLOTS, :],
                                                   w[rows, c:c + HALF].bitcast(F32), SUBTRACT)
                last.then_inc(w_low_ready, 1)

            def tile(t, buffer, first, last):
                dve.wait_ge(x_landed[buffer], x_landings(t, buffer))
                for u, (unit, _, _) in enumerate(UNITS):
                    if first:
                        for k in chunks_asked_at(u):
                            split_w_low(k)
                    dve.wait_ge(unit_multiplied, t * N + u + 1)
                    if not first or u >= STAGES:
                        dve.wait_ge(stored[u % STAGES], (t * ROUNDS + u // STAGES) * 16)
                    col = 0
                    for _, j, pairs in unit:
                        n = pairs * EMBED
                        done = nc.vector.tensor_tensor(stage[:, u % STAGES, col:col + n],
                                                       products[u % PSUM_SLOTS][:, col:col + n],
                                                       x_rows[:, buffer, j * EMBED:j * EMBED + n], MULT)
                        col += n
                    done.then_inc(unit_done, 1)

            over_tiles(dve, tile)


def kernel(r_feature_emb, L0_rec_W):
    import numpy as np
    import concourse.bacc as bacc
    from concourse.bass_utils import run_bass_kernel_spmd

    x = np.ascontiguousarray(r_feature_emb).reshape(BATCH, FIELDS * EMBED)
    w = np.asarray(L0_rec_W).reshape(CHUNKS, 2, HALF, EMBED)
    wt = np.ascontiguousarray(w.transpose(1, 3, 0, 2)).reshape(P, COLS // 2)

    nc = bacc.Bacc("TRN2", target_bir_lowering=False, num_devices=1)
    x_dram = nc.dram_tensor("x", x.shape, F32, kind="ExternalInput").ap()
    wt_dram = nc.dram_tensor("wt", wt.shape, F32, kind="ExternalInput").ap()
    out_dram = nc.dram_tensor("out", (BATCH, COLS), F32, kind="ExternalOutput").ap()
    build(nc, x_dram, wt_dram, out_dram)
    result = run_bass_kernel_spmd(nc, [{"x": x, "wt": wt}], core_ids=[0])
    return result.results[0]["out"].reshape(BATCH, PAIRS, EMBED)
```

```python
from contextlib import ExitStack

import concourse.bass as bass
from concourse import mybir

F32 = mybir.dt.float32
F32R = mybir.dt.float32r
MULT = mybir.AluOpType.mult
SUBTRACT = mybir.AluOpType.subtract
NOT_EQUAL = mybir.AluOpType.not_equal
COPY = mybir.ActivationFunctionType.Copy

P = 128
BATCH, FIELDS, EMBED = 4096, 32, 64
TILES = BATCH // P
PAIRS = FIELDS * (FIELDS - 1) // 2
COLS = PAIRS * EMBED
BANK = 512

HALF = 512
CHUNK = 2 * HALF
CHUNKS = COLS // CHUNK

UNIT_PAIRS = 3 * BANK // EMBED
UNIT_COLS = UNIT_PAIRS * EMBED
PSUM_SLOTS = 2
STAGES = 5
RAW_SLOTS = 5

GROUPS = FIELDS // 2
TURN_SLOTS = 2
XT_SLOTS = 4

AHEAD_GROUP = 1
AHEAD_W = 2
CHUNKS_AT_ONCE = 2
SPLIT_LOWER_AT = 20
SPLIT_UPPER_AT = 1


def first_pair(i):
    return i * (FIELDS - 1) - i * (i - 1) // 2


def plan():
    units = []
    for i in range(FIELDS - 1):
        pairs = FIELDS - 1 - i
        if pairs > UNIT_PAIRS:
            first = (pairs + 1) // 2
            units += [[(i, i + 1, first)], [(i, i + 1 + first, pairs - first)]]
        elif sum(p[2] for p in units[-1]) + pairs <= UNIT_PAIRS and pairs < UNIT_PAIRS // 2 + 1:
            units[-1].append((i, i + 1, pairs))
        else:
            units.append([(i, i + 1, pairs)])
    start = [first_pair(u[0][0]) + u[0][1] - u[0][0] - 1 for u in units] + [PAIRS]
    return [(u, s * EMBED, (e - s) * EMBED) for u, s, e in zip(units, start, start[1:])]


UNITS = plan()
N = len(UNITS)
assert N % PSUM_SLOTS == 0 and N % STAGES == 0 and GROUPS % XT_SLOTS == 0
ROUNDS = N // STAGES

FIRST_UNIT_OF_GROUP = [min(u for u in range(N) for p in UNITS[u][0] if p[0] // 2 == g)
                       for g in range(GROUPS)]
LAST_UNIT_OF_GROUP = [max(u for u in range(N) for p in UNITS[u][0] if p[0] // 2 == g)
                      for g in range(GROUPS)]
FIRST_UNIT_OF_CHUNK = [max(u for u in range(N) if UNITS[u][1] <= k * CHUNK) for k in range(CHUNKS)]
LAST_CHUNK_OF_UNIT = [(UNITS[u][1] + UNITS[u][2] - 1) // CHUNK for u in range(N)]


def groups_asked_at(u):
    ahead, v = divmod(u + AHEAD_GROUP, N)
    return [(ahead, g) for g in range(GROUPS) if FIRST_UNIT_OF_GROUP[g] == v]


assert SPLIT_LOWER_AT >= FIRST_UNIT_OF_GROUP[GROUPS // 2 - 1] - AHEAD_GROUP


def groups_asked_before():
    return [g for g in range(GROUPS) if FIRST_UNIT_OF_GROUP[g] < AHEAD_GROUP]


def chunks_asked_at(u):
    return [k for k in range(CHUNKS_AT_ONCE, CHUNKS) if max(FIRST_UNIT_OF_CHUNK[k] - AHEAD_W, 0) == u]


def group_fields(g):
    return [i for i in (2 * g, 2 * g + 1) if i < FIELDS - 1]


def matmul_pieces(unit, start):
    pieces, col = [], 0
    for i, _, pairs in unit:
        end, stretches = col + pairs * EMBED, []
        while col < end:
            n = min(end, (col // BANK + 1) * BANK) - col
            stretches.append((col, start + col, n))
            col += n
        pieces.append((i, stretches))
    return pieces


def build(nc, x, wt, out):
    with ExitStack() as ctx:
        def sbuf(name, shape, dtype=F32):
            return ctx.enter_context(nc.sbuf_tensor(name, shape, dtype))

        def psum(name, cols):
            return ctx.enter_context(nc.psum_tensor(name, [P, cols], F32))

        def sem(name):
            return ctx.enter_context(nc.semaphore(name))

        w = sbuf("w", [P, COLS], F32R)
        w_raw = sbuf("w_raw", [P, RAW_SLOTS, HALF])
        x_rows = sbuf("x_rows", [P, 2, FIELDS * EMBED])
        x_parts = sbuf("x_parts", [P, FIELDS, 2, EMBED], F32R)
        x_turned = sbuf("x_turned", [P, XT_SLOTS, 2, 2, P], F32R)
        stage = sbuf("stage", [P, STAGES, UNIT_COLS])
        identity = sbuf("identity", [P, P])
        products = [psum(f"products{s}", UNIT_COLS) for s in range(PSUM_SLOTS)]
        turned = [psum(f"turned{s}", BANK)[:, 0:2 * P].rearrange("p (i b) -> p i b", i=2)
                  for s in range(TURN_SLOTS)]

        x_group0_landed = sem("x_group0_landed")
        x_landed = [sem(f"x_landed{s}") for s in range(2)]
        w_landed = [sem(f"w_landed{s}") for s in range(RAW_SLOTS)]
        identity_zeroed = sem("identity_zeroed")
        identity_ready = sem("identity_ready")
        w_high_ready = sem("w_high_ready")
        w_low_ready = sem("w_low_ready")
        x_high_ready = sem("x_high_ready")
        x_low_ready = sem("x_low_ready")
        group_turned = sem("group_turned")
        group_ready = sem("group_ready")
        unit_multiplied = sem("unit_multiplied")
        unit_done = sem("unit_done")
        stored = [sem(f"stored{s}") for s in range(STAGES)]

        block = ctx.enter_context(nc.Block())

        def over_tiles(engine, step):
            step(0, 0, True, False)
            with engine.Fori(0, (TILES - 2) // 2) as n:
                step(2 * n + 1, 1, False, False)
                step(2 * n + 2, 0, False, False)
            step(TILES - 1, 1, False, True)

        def x_landings(t, buffer):
            return (t - buffer) * 8 + 16

        def splits(t, half):
            return 2 * t + half + 2

        def fields_of(half):
            return half * FIELDS // 2, (half + 1) * FIELDS // 2

        @block.sync
        def _(sp):
            def load_x(t, buffer):
                sp.dma_start(x_rows[:, buffer, :], x[bass.ds(t * P, P), :]).then_inc(x_landed[buffer], 16)

            def load_w(k):
                if k >= RAW_SLOTS:
                    sp.wait_ge(w_low_ready, k - RAW_SLOTS + 1)
                sp.dma_start(w_raw[:, k % RAW_SLOTS, :], wt[:, k * HALF:(k + 1) * HALF]) \
                    .then_inc(w_landed[k % RAW_SLOTS], 16)

            def tile(t, buffer, first, last):
                for u, (_, start, cols) in enumerate(UNITS):
                    if first:
                        for k in chunks_loaded_at(u):
                            load_w(k)
                    sp.wait_ge(unit_done, t * N + u + 1)
                    sp.dma_start(out[bass.ds(t * P, P), start:start + cols], stage[:, u % STAGES, 0:cols]) \
                        .then_inc(stored[u % STAGES], 16)
                    if u == 0 and not last:
                        load_x(t + 1, 1 - buffer)

            def chunks_loaded_at(u):
                ks = chunks_asked_at(u)
                return [k + RAW_SLOTS for k in (ks if u else [*range(CHUNKS_AT_ONCE), *ks])
                        if k + RAW_SLOTS < CHUNKS]

            sp.dma_start(x_rows[:, 0, 0:2 * EMBED], x[0:P, 0:2 * EMBED]).then_inc(x_group0_landed, 16)
            load_w(0)
            sp.dma_start(x_rows[:, 0, 2 * EMBED:], x[0:P, 2 * EMBED:]).then_inc(x_landed[0], 16)
            for k in range(1, RAW_SLOTS):
                load_w(k)
            over_tiles(sp, tile)
            for s in range(STAGES):
                sp.wait_ge(stored[s], 16 * ROUNDS * TILES)

        @block.gpsimd
        def _(pool):
            nc.gpsimd.memset(identity[:, :], 0.0).then_inc(identity_zeroed, 1)
            pool.wait_ge(identity_zeroed, 1)
            nc.gpsimd.affine_select(out=identity[:, :], in_=identity[:, :], compare_op=NOT_EQUAL, fill=1.0,
                                    base=0, pattern=[[-1, P]], channel_multiplier=1).then_inc(identity_ready, 1)

            def split_low(buffer, a, b, highs):
                pool.wait_ge(x_high_ready, highs)
                nc.gpsimd.tensor_tensor(
                    x_parts[:, a:b, 1, :].bitcast(F32),
                    x_rows[:, buffer, a * EMBED:b * EMBED].rearrange("p (i e) -> p i e", e=EMBED),
                    x_parts[:, a:b, 0, :].bitcast(F32), SUBTRACT).then_inc(x_low_ready, 1)

            def tile(t, buffer, first, last):
                split_low(buffer, *fields_of(1), splits(t, 1))
                if not last:
                    split_low(1 - buffer, *fields_of(0), splits(t + 1, 0))

            split_low(0, 0, 2, 1)
            split_low(0, 2, FIELDS // 2, splits(0, 0))
            over_tiles(pool, tile)

        @block.scalar
        def _(act):
            def split_high(buffer, a, b):
                nc.scalar.activation(
                    x_parts[:, a:b, 0, :],
                    x_rows[:, buffer, a * EMBED:b * EMBED].rearrange("p (i e) -> p i e", e=EMBED),
                    COPY).then_inc(x_high_ready, 1)

            def split_high_half(t, buffer, half, first):
                act.wait_ge(x_landed[buffer], x_landings(t, buffer))
                if not first:
                    act.wait_ge(group_turned, (t - 1) * GROUPS + (half + 1) * GROUPS // 2)
                split_high(buffer, *fields_of(half))

            def evacuate(t, g, first):
                act.wait_ge(group_turned, t * GROUPS + g + 1)
                if not first:
                    behind, before = divmod(g - XT_SLOTS, GROUPS)
                    act.wait_ge(unit_multiplied, (t + behind) * N + LAST_UNIT_OF_GROUP[before] + 1)
                n = len(group_fields(g))
                high, low = slice(0, EMBED), slice(EMBED, P)
                for rows, swapped, source in ((slice(0, P), 0, slice(0, P)), (high, 1, low), (low, 1, high)):
                    nc.scalar.activation(x_turned[rows, g % XT_SLOTS, swapped, 0:n, :],
                                         turned[g % TURN_SLOTS][source, 0:n, :], COPY) \
                        .then_inc(group_ready, 1)

            def round_w(k):
                act.wait_ge(w_landed[k % RAW_SLOTS], 16 * (k // RAW_SLOTS + 1))
                for half in range(2):
                    rows = slice(half * EMBED, (half + 1) * EMBED)
                    c = k * CHUNK + half * HALF
                    nc.scalar.activation(w[rows, c:c + HALF], w_raw[rows, k % RAW_SLOTS, :], COPY) \
                        .then_inc(w_high_ready, 1)

            def tile(t, buffer, first, last):
                for u in range(N):
                    for ahead, g in groups_asked_at(u):
                        if not (last and ahead):
                            evacuate(t + ahead, g, first and not ahead and g < XT_SLOTS)
                    if first:
                        for k in chunks_asked_at(u):
                            round_w(k)
                    if u == SPLIT_UPPER_AT:
                        split_high_half(t, buffer, 1, first)
                    if u == SPLIT_LOWER_AT and not last:
                        split_high_half(t + 1, 1 - buffer, 0, False)

            act.wait_ge(x_group0_landed, 16)
            split_high(0, 0, 2)
            round_w(0)
            for g in groups_asked_before():
                evacuate(0, g, True)
            act.wait_ge(x_landed[0], x_landings(0, 0))
            split_high(0, 2, FIELDS // 2)
            for k in range(1, CHUNKS_AT_ONCE):
                round_w(k)
            over_tiles(act, tile)

        @block.tensor
        def _(pe):
            def transpose(t, g, first):
                if first and g == 0:
                    pe.wait_ge(x_low_ready, 1)
                elif g in (0, GROUPS // 2) or first and g == 1:
                    pe.wait_ge(x_low_ready, splits(t, g // (GROUPS // 2)))
                if not first or g >= TURN_SLOTS:
                    pe.wait_ge(group_ready, 3 * (t * GROUPS + g - TURN_SLOTS + 1))
                for n, i in enumerate(group_fields(g)):
                    parts = x_parts[:, i, :, :].bitcast(F32).rearrange("p s e -> p (s e)")
                    last = nc.tensor.transpose(turned[g % TURN_SLOTS][:, n, :], parts, identity[:, :])
                last.then_inc(group_turned, 1)

            def multiply(t, u, first):
                unit, start, _ = UNITS[u]
                for g in range(GROUPS):
                    if FIRST_UNIT_OF_GROUP[g] == u:
                        pe.wait_ge(group_ready, 3 * (t * GROUPS + g + 1))
                if first:
                    pe.wait_ge(w_low_ready, LAST_CHUNK_OF_UNIT[u] + 1)
                if not first or u >= PSUM_SLOTS:
                    pe.wait_ge(unit_done, t * N + u - PSUM_SLOTS + 1)
                slot = products[u % PSUM_SLOTS]
                for i, stretches in matmul_pieces(unit, start):
                    for swapped in range(2):
                        weights = x_turned[:, i // 2 % XT_SLOTS, swapped, i % 2, :]
                        for c, wc, n in stretches:
                            last = nc.tensor.matmul(slot[:, c:c + n], weights, w[:, wc:wc + n],
                                                    start=(swapped == 0), stop=(swapped == 1))
                last.then_inc(unit_multiplied, 1)

            def tile(t, buffer, first, last):
                for u in range(N):
                    for ahead, g in groups_asked_at(u):
                        if not (last and ahead):
                            transpose(t + ahead, g, first and not ahead)
                    multiply(t, u, first)

            pe.wait_ge(identity_ready, 1)
            for g in groups_asked_before():
                transpose(0, g, True)
            over_tiles(pe, tile)

        @block.vector
        def _(dve):
            def split_w_low(k):
                for half in range(2):
                    rows = slice(half * EMBED, (half + 1) * EMBED)
                    across = slice((1 - half) * EMBED, (2 - half) * EMBED)
                    c = k * CHUNK + half * HALF
                    dve.wait_ge(w_high_ready, 2 * k + half + 1)
                    last = nc.vector.tensor_tensor(w[across, c:c + HALF], w_raw[rows, k % RAW_SLOTS, :],
                                                   w[rows, c:c + HALF].bitcast(F32), SUBTRACT)
                last.then_inc(w_low_ready, 1)

            def tile(t, buffer, first, last):
                if first:
                    for k in range(CHUNKS_AT_ONCE):
                        split_w_low(k)
                    dve.wait_ge(x_group0_landed, 16)
                dve.wait_ge(x_landed[buffer], x_landings(t, buffer))
                for u, (unit, _, _) in enumerate(UNITS):
                    if first:
                        for k in chunks_asked_at(u):
                            split_w_low(k)
                    dve.wait_ge(unit_multiplied, t * N + u + 1)
                    if not first or u >= STAGES:
                        dve.wait_ge(stored[u % STAGES], (t * ROUNDS + u // STAGES) * 16)
                    col = 0
                    for _, j, pairs in unit:
                        n = pairs * EMBED
                        done = nc.vector.tensor_tensor(stage[:, u % STAGES, col:col + n],
                                                       products[u % PSUM_SLOTS][:, col:col + n],
                                                       x_rows[:, buffer, j * EMBED:j * EMBED + n], MULT)
                        col += n
                    done.then_inc(unit_done, 1)

            over_tiles(dve, tile)


def kernel(r_feature_emb, L0_rec_W):
    import numpy as np
    import concourse.bacc as bacc
    from concourse.bass_utils import run_bass_kernel_spmd

    x = np.ascontiguousarray(r_feature_emb).reshape(BATCH, FIELDS * EMBED)
    w = np.asarray(L0_rec_W).reshape(CHUNKS, 2, HALF, EMBED)
    wt = np.ascontiguousarray(w.transpose(1, 3, 0, 2)).reshape(P, COLS // 2)

    nc = bacc.Bacc("TRN2", target_bir_lowering=False, num_devices=1)
    x_dram = nc.dram_tensor("x", x.shape, F32, kind="ExternalInput").ap()
    wt_dram = nc.dram_tensor("wt", wt.shape, F32, kind="ExternalInput").ap()
    out_dram = nc.dram_tensor("out", (BATCH, COLS), F32, kind="ExternalOutput").ap()
    build(nc, x_dram, wt_dram, out_dram)
    result = run_bass_kernel_spmd(nc, [{"x": x, "wt": wt}], core_ids=[0])
    return result.results[0]["out"].reshape(BATCH, PAIRS, EMBED)
```
